# Optimizing a Trainium2 kernel written in Bass

```python
import numpy as np
import jax
import jax.numpy as jnp

def _softmax(x, axis=-1):
    return jax.nn.softmax(x, axis=axis)

def _gelu(x):
    return jax.nn.gelu(x, approximate=True)

def _silu(x):
    return jax.nn.silu(x)

def _sigmoid(x):
    return jax.nn.sigmoid(x)

def _layernorm(x, axis=-1, eps=1e-05):
    m = jnp.mean(x, axis=axis, keepdims=True)
    v = jnp.var(x, axis=axis, keepdims=True)
    return (x - m) / jnp.sqrt(v + eps)

def _scatter_add(tgt, idx, src, axis=0):
    return tgt.at[idx].add(src)

def _segment_sum(src, seg, n):
    return jax.ops.segment_sum(src, seg, n)
kernel_name = 'mk_gnn_resnorm_d4_gnn_r32_a5f7eb'

def setup_inputs(seed: int=0):
    np.random.seed(seed)
    _w = jnp.asarray

    def _rec_inputs():
        import jax
        import jax.numpy as jnp
        _gk = jax.random.key(seed)
        x = -0.000202 + 1 * jax.random.normal(jax.random.fold_in(_gk, 1), (3125, 128), jnp.float32)
        src = jax.random.randint(jax.random.fold_in(_gk, 2), (50000,), 0, 3125, jnp.int32)
        dst = jnp.minimum((3125 * jax.random.uniform(jax.random.fold_in(_gk, 3), (50000,)) ** 2.0).astype(jnp.int32), 99999)
        _o = jnp.argsort(dst, stable=True)
        src = src[_o]
        dst = dst[_o]
        edge_attr_128 = -8.16379e-05 + 0.999858 * jax.random.normal(jax.random.fold_in(_gk, 12), (50000, 128), jnp.float32)
        edge_type_6 = jax.random.randint(jax.random.fold_in(_gk, 14), (50000,), 0, 6, jnp.int32)
        edge_weight1 = 0.000452788 + 0.999756 * jax.random.normal(jax.random.fold_in(_gk, 15), (50000, 1), jnp.float32)
        node_type_3 = jax.random.randint(jax.random.fold_in(_gk, 16), (3125,), 0, 3, jnp.int32)
        return (x, src, dst, edge_attr_128, edge_type_6, edge_weight1, node_type_3)
    x, src, dst, edge_attr_128, edge_type_6, edge_weight1, node_type_3 = _rec_inputs()

    def _L0_gnn_setup():
        import jax, jax.numpy as jnp
        import numpy as np
        N, D, H, HD = (50000, 128, 8, 16)
        E = 25000
        NT, ET, L = (3, 6, 2)
        SQRT_D = float(np.sqrt(HD))

        def typed_linear(x, tids, W):
            out = jnp.zeros((x.shape[0], W.shape[-1]), x.dtype)
            for t in range(W.shape[0]):
                out = out + jnp.where((tids == t)[:, None], x @ W[t], 0.0)
            return out

        def hgt_layer(x, ntype, src, dst, etype, Wk, Wq, Wv, Wa, pri, Watt, Wmsg, skip):
            n = x.shape[0]
            k = typed_linear(x, ntype, Wk).reshape(n, H, HD)
            q = typed_linear(x, ntype, Wq).reshape(n, H, HD)
            v = typed_linear(x, ntype, Wv).reshape(n, H, HD)
            k_e, q_e, v_e = (k[src], q[dst], v[src])
            kw = jnp.zeros_like(k_e)
            mv = jnp.zeros_like(v_e)
            for t in range(ET):
                m = (etype == t)[:, None, None]
                kw = kw + jnp.where(m, jnp.einsum('ehd,hdo->eho', k_e, Watt[:, t]), 0.0)
                mv = mv + jnp.where(m, jnp.einsum('ehd,hdo->eho', v_e, Wmsg[:, t]), 0.0)
            a = jnp.sum(kw * q_e, axis=-1) * pri.T[etype] / SQRT_D
            amax = jax.ops.segment_max(a, dst, num_segments=n)
            amax = jnp.where(jnp.isfinite(amax), amax, 0.0)
            ea = jnp.exp(a - amax[dst])
            esum = jax.ops.segment_sum(ea, dst, num_segments=n)
            attn = ea / esum[dst]
            msg = (mv * attn[:, :, None]).reshape(-1, H * HD)
            h = jax.ops.segment_sum(msg, dst, num_segments=n)
            h = typed_linear(h, ntype, Wa)
            alpha = jax.nn.sigmoid(skip)[ntype][:, None]
            return h * alpha + x * (1.0 - alpha)
        key = jax.random.key(seed)
        ks = jax.random.split(key, 12)
        x = jax.random.normal(ks[0], (N, D), dtype=jnp.float32)
        ntype = jnp.sort(jax.random.randint(ks[1], (N,), 0, NT))
        src = jax.random.randint(ks[2], (E,), 0, N)
        dst = jax.random.randint(ks[3], (E,), 0, N)
        etype = jnp.sort(jax.random.randint(ks[4], (E,), 0, ET))
        s = 1.0 / np.sqrt(D)
        Wk = jax.random.normal(ks[5], (L, NT, D, D), dtype=jnp.float32) * s
        Wq = jax.random.normal(ks[6], (L, NT, D, D), dtype=jnp.float32) * s
        Wv = jax.random.normal(ks[7], (L, NT, D, D), dtype=jnp.float32) * s
        Wa = jax.random.normal(ks[8], (L, NT, D, D), dtype=jnp.float32) * s
        sh = 1.0 / np.sqrt(HD)
        Watt = jax.random.normal(ks[9], (L, H, ET, HD, HD), dtype=jnp.float32) * sh
        Wmsg = jax.random.normal(ks[10], (L, H, ET, HD, HD), dtype=jnp.float32) * sh
        pri = jnp.ones((L, H, ET), dtype=jnp.float32)
        skip = jnp.ones((L, NT), dtype=jnp.float32)
        return dict(x=x, ntype=ntype, src=src, dst=dst, etype=etype, Wk=Wk, Wq=Wq, Wv=Wv, Wa=Wa, pri=pri, Watt=Watt, Wmsg=Wmsg, skip=skip)
    _L0_gnn_all = _L0_gnn_setup()
    _L0_gnn_in = {k: v for k, v in _L0_gnn_all.items() if k in ('Wk', 'Wq', 'Wv', 'Wa', 'pri', 'Watt', 'Wmsg', 'skip')}
    del _L0_gnn_all

    def _L1_gnn_setup():
        import jax, jax.numpy as jnp
        import numpy as np
        N_NODES = 3125
        N_EDGES = 50000
        D = 128
        key = jax.random.key(seed)
        ks = jax.random.split(key, 10)
        s = 1.0 / np.sqrt(D)
        return {'x': jax.random.normal(ks[0], (N_NODES, D), dtype=jnp.float32), 'edge_index': jax.random.randint(ks[1], (2, N_EDGES), 0, N_NODES, dtype=jnp.int64), 'edge_attr': jax.random.normal(ks[2], (N_EDGES, 1), dtype=jnp.float32), 'W1l': jax.random.normal(ks[3], (D, D), dtype=jnp.float32) * s, 'b1': jnp.zeros((D,), dtype=jnp.float32), 'W1r': jax.random.normal(ks[4], (D, D), dtype=jnp.float32) * s, 'W2l': jax.random.normal(ks[5], (D, D), dtype=jnp.float32) * s, 'b2': jnp.zeros((D,), dtype=jnp.float32), 'W2r': jax.random.normal(ks[6], (D, D), dtype=jnp.float32) * s, 'W3l': jax.random.normal(ks[7], (D, D), dtype=jnp.float32) * s, 'b3': jnp.zeros((D,), dtype=jnp.float32), 'W3r': jax.random.normal(ks[8], (D, D), dtype=jnp.float32) * s}
    _L1_gnn_all = _L1_gnn_setup()
    _L1_gnn_in = {k: v for k, v in _L1_gnn_all.items() if k in ('W1l', 'b1', 'W1r', 'W2l', 'b2', 'W2r', 'W3l', 'b3', 'W3r')}
    del _L1_gnn_all

    def _L2_gnn_setup():
        import jax, jax.numpy as jnp
        import numpy as np
        key = jax.random.key(seed)
        k1, k2, k3, k4 = jax.random.split(key, 4)
        N, E, F_IN, F_OUT = (50000, 25000, 128, 128)
        x = jax.random.normal(k1, (N, F_IN), dtype=jnp.float32)
        src = jax.random.randint(k2, (E,), 0, N, dtype=jnp.int32)
        dst = jax.random.randint(k3, (E,), 0, N, dtype=jnp.int32)
        W = jax.random.normal(k4, (F_OUT, 2 * F_IN), dtype=jnp.float32) * (1.0 / np.sqrt(2 * F_IN))
        return {'x': x, 'src': src, 'dst': dst, 'num_nodes': N, 'W': W}
    _L2_gnn_all = _L2_gnn_setup()
    _L2_gnn_in = {k: v for k, v in _L2_gnn_all.items() if k in ('W',)}
    del _L2_gnn_all

    def _L3_gnn_setup():
        import jax, jax.numpy as jnp
        import numpy as np
        N, E, H, T = (50000, 25000, 128, 2)

        def _gru_cell(x, h, Wih, Whh, bih, bhh):
            gi = x @ Wih.T + bih
            gh = h @ Whh.T + bhh
            ir, iz, inn = jnp.split(gi, 3, axis=1)
            hr, hz, hn = jnp.split(gh, 3, axis=1)
            r = jax.nn.sigmoid(ir + hr)
            z = jax.nn.sigmoid(iz + hz)
            n = jnp.tanh(inn + r * hn)
            return (1.0 - z) * n + z * h
        key = jax.random.key(seed)
        ks = jax.random.split(key, 16)
        inp = {'h': jax.random.normal(ks[0], (N, H), dtype=jnp.float32), 'e': jax.random.normal(ks[1], (E, H), dtype=jnp.float32), 'src': jax.random.randint(ks[2], (E,), 0, N), 'dst': jax.random.randint(ks[3], (E,), 0, N)}
        i = 4
        for t in range(T):
            inp[f'W_msg_{t}'] = jax.random.normal(ks[i], (2 * H, 3 * H), dtype=jnp.float32) * 0.05
            i += 1
            inp[f'b_msg_{t}'] = jnp.zeros((2 * H,), jnp.float32)
            inp[f'Wih_{t}'] = jax.random.normal(ks[i], (3 * H, 2 * H), dtype=jnp.float32) * 0.05
            i += 1
            inp[f'Whh_{t}'] = jax.random.normal(ks[i], (3 * H, H), dtype=jnp.float32) * 0.05
            i += 1
            inp[f'bih_{t}'] = jnp.zeros((3 * H,), jnp.float32)
            inp[f'bhh_{t}'] = jnp.zeros((3 * H,), jnp.float32)
        return inp
    _L3_gnn_all = _L3_gnn_setup()
    _L3_gnn_in = {k: v for k, v in _L3_gnn_all.items() if k in ('W_msg_0', 'b_msg_0', 'Wih_0', 'Whh_0', 'bih_0', 'bhh_0', 'W_msg_1', 'b_msg_1', 'Wih_1', 'Whh_1', 'bih_1', 'bhh_1')}
    del _L3_gnn_all
    return {'x': x, 'src': src, 'dst': dst, 'edge_attr_128': edge_attr_128, 'edge_type_6': edge_type_6, 'edge_weight1': edge_weight1, 'node_type_3': node_type_3, 'L0_gnn_Wk': _L0_gnn_in['Wk'], 'L0_gnn_Wq': _L0_gnn_in['Wq'], 'L0_gnn_Wv': _L0_gnn_in['Wv'], 'L0_gnn_Wa': _L0_gnn_in['Wa'], 'L0_gnn_pri': _L0_gnn_in['pri'], 'L0_gnn_Watt': _L0_gnn_in['Watt'], 'L0_gnn_Wmsg': _L0_gnn_in['Wmsg'], 'L0_gnn_skip': _L0_gnn_in['skip'], 'L1_gnn_W1l': _L1_gnn_in['W1l'], 'L1_gnn_b1': _L1_gnn_in['b1'], 'L1_gnn_W1r': _L1_gnn_in['W1r'], 'L1_gnn_W2l': _L1_gnn_in['W2l'], 'L1_gnn_b2': _L1_gnn_in['b2'], 'L1_gnn_W2r': _L1_gnn_in['W2r'], 'L1_gnn_W3l': _L1_gnn_in['W3l'], 'L1_gnn_b3': _L1_gnn_in['b3'], 'L1_gnn_W3r': _L1_gnn_in['W3r'], 'L2_gnn_W': _L2_gnn_in['W'], 'L3_gnn_W_msg_0': _L3_gnn_in['W_msg_0'], 'L3_gnn_b_msg_0': _L3_gnn_in['b_msg_0'], 'L3_gnn_Wih_0': _L3_gnn_in['Wih_0'], 'L3_gnn_Whh_0': _L3_gnn_in['Whh_0'], 'L3_gnn_bih_0': _L3_gnn_in['bih_0'], 'L3_gnn_bhh_0': _L3_gnn_in['bhh_0'], 'L3_gnn_W_msg_1': _L3_gnn_in['W_msg_1'], 'L3_gnn_b_msg_1': _L3_gnn_in['b_msg_1'], 'L3_gnn_Wih_1': _L3_gnn_in['Wih_1'], 'L3_gnn_Whh_1': _L3_gnn_in['Whh_1'], 'L3_gnn_bih_1': _L3_gnn_in['bih_1'], 'L3_gnn_bhh_1': _L3_gnn_in['bhh_1']}

def reference(x, src, dst, edge_attr_128, edge_type_6, edge_weight1, node_type_3, L0_gnn_Wk, L0_gnn_Wq, L0_gnn_Wv, L0_gnn_Wa, L0_gnn_pri, L0_gnn_Watt, L0_gnn_Wmsg, L0_gnn_skip, L1_gnn_W1l, L1_gnn_b1, L1_gnn_W1r, L1_gnn_W2l, L1_gnn_b2, L1_gnn_W2r, L1_gnn_W3l, L1_gnn_b3, L1_gnn_W3r, L2_gnn_W, L3_gnn_W_msg_0, L3_gnn_b_msg_0, L3_gnn_Wih_0, L3_gnn_Whh_0, L3_gnn_bih_0, L3_gnn_bhh_0, L3_gnn_W_msg_1, L3_gnn_b_msg_1, L3_gnn_Wih_1, L3_gnn_Whh_1, L3_gnn_bih_1, L3_gnn_bhh_1):
    import jax
    import jax.numpy as jnp

    def _L0_gnn_ref(x, ntype, src, dst, etype, Wk, Wq, Wv, Wa, pri, Watt, Wmsg, skip):
        import jax, jax.numpy as jnp
        import numpy as np
        N, D, H, HD = (50000, 128, 8, 16)
        E = 25000
        NT, ET, L = (3, 6, 2)
        SQRT_D = float(np.sqrt(HD))

        def typed_linear(x, tids, W):
            out = jnp.zeros((x.shape[0], W.shape[-1]), x.dtype)
            for t in range(W.shape[0]):
                out = out + jnp.where((tids == t)[:, None], x @ W[t], 0.0)
            return out

        def hgt_layer(x, ntype, src, dst, etype, Wk, Wq, Wv, Wa, pri, Watt, Wmsg, skip):
            n = x.shape[0]
            k = typed_linear(x, ntype, Wk).reshape(n, H, HD)
            q = typed_linear(x, ntype, Wq).reshape(n, H, HD)
            v = typed_linear(x, ntype, Wv).reshape(n, H, HD)
            k_e, q_e, v_e = (k[src], q[dst], v[src])
            kw = jnp.zeros_like(k_e)
            mv = jnp.zeros_like(v_e)
            for t in range(ET):
                m = (etype == t)[:, None, None]
                kw = kw + jnp.where(m, jnp.einsum('ehd,hdo->eho', k_e, Watt[:, t]), 0.0)
                mv = mv + jnp.where(m, jnp.einsum('ehd,hdo->eho', v_e, Wmsg[:, t]), 0.0)
            a = jnp.sum(kw * q_e, axis=-1) * pri.T[etype] / SQRT_D
            amax = jax.ops.segment_max(a, dst, num_segments=n)
            amax = jnp.where(jnp.isfinite(amax), amax, 0.0)
            ea = jnp.exp(a - amax[dst])
            esum = jax.ops.segment_sum(ea, dst, num_segments=n)
            attn = ea / esum[dst]
            msg = (mv * attn[:, :, None]).reshape(-1, H * HD)
            h = jax.ops.segment_sum(msg, dst, num_segments=n)
            h = typed_linear(h, ntype, Wa)
            alpha = jax.nn.sigmoid(skip)[ntype][:, None]
            return h * alpha + x * (1.0 - alpha)
        h = x
        for l in range(L):
            h = hgt_layer(h, ntype, src, dst, etype, Wk[l], Wq[l], Wv[l], Wa[l], pri[l], Watt[l], Wmsg[l], skip[l])
        return h

    def _L1_gnn_ref(x, edge_index, edge_attr, W1l, b1, W1r, W2l, b2, W2r, W3l, b3, W3r):
        import jax, jax.numpy as jnp
        import numpy as np
        N_NODES = 3125
        N_EDGES = 50000
        D = 128
        src, dst = (edge_index[0], edge_index[1])
        n = x.shape[0]
        deg = jax.ops.segment_sum(jnp.ones_like(dst, dtype=x.dtype), dst, num_segments=n)
        deg_inv = 1.0 / jnp.maximum(deg, 1.0)

        def sage(h, Wl, bl, Wr):
            agg = jax.ops.segment_sum(h[src], dst, num_segments=n) * deg_inv[:, None]
            return agg @ Wl.T + bl + h @ Wr.T
        h = jax.nn.relu(sage(x, W1l, b1, W1r))
        h = jax.nn.relu(sage(h, W2l, b2, W2r))
        return sage(h, W3l, b3, W3r)

    def _L2_gnn_ref(x, src, dst, num_nodes, W):
        import jax, jax.numpy as jnp
        import numpy as np
        msgs = x[src]
        summed = jax.ops.segment_sum(msgs, dst, num_segments=num_nodes)
        deg = jax.ops.segment_sum(jnp.ones_like(dst, dtype=x.dtype), dst, num_segments=num_nodes)
        agg = summed / jnp.maximum(deg, 1.0)[:, None]
        h = jnp.concatenate([x, agg], axis=1)
        out = h @ W.T
        return jax.nn.relu(out)

    def _L3_gnn_ref(h, e, src, dst, W_msg_0, b_msg_0, Wih_0, Whh_0, bih_0, bhh_0, W_msg_1, b_msg_1, Wih_1, Whh_1, bih_1, bhh_1):
        import jax, jax.numpy as jnp
        import numpy as np
        N, E, H, T = (50000, 25000, 128, 2)

        def _gru_cell(x, h, Wih, Whh, bih, bhh):
            gi = x @ Wih.T + bih
            gh = h @ Whh.T + bhh
            ir, iz, inn = jnp.split(gi, 3, axis=1)
            hr, hz, hn = jnp.split(gh, 3, axis=1)
            r = jax.nn.sigmoid(ir + hr)
            z = jax.nn.sigmoid(iz + hz)
            n = jnp.tanh(inn + r * hn)
            return (1.0 - z) * n + z * h
        params = [(W_msg_0, b_msg_0, Wih_0, Whh_0, bih_0, bhh_0), (W_msg_1, b_msg_1, Wih_1, Whh_1, bih_1, bhh_1)]
        n_nodes = h.shape[0]
        deg = jax.ops.segment_sum(jnp.ones((dst.shape[0],), h.dtype), dst, num_segments=n_nodes)
        denom = jnp.maximum(deg, 1.0)[:, None]
        for Wm, bm, Wih, Whh, bih, bhh in params:
            msg_in = jnp.concatenate([h[dst], h[src], e], axis=1)
            act_e = msg_in @ Wm.T + bm
            a = jax.ops.segment_sum(act_e, dst, num_segments=n_nodes) / denom
            h = _gru_cell(a, h, Wih, Whh, bih, bhh)
        return h
    edge_index = jnp.stack([src, dst])
    x = _layernorm(x + _L0_gnn_ref(x, node_type_3, src, dst, edge_type_6, L0_gnn_Wk, L0_gnn_Wq, L0_gnn_Wv, L0_gnn_Wa, L0_gnn_pri, L0_gnn_Watt, L0_gnn_Wmsg, L0_gnn_skip), axis=-1)
    x = _layernorm(x + _L1_gnn_ref(x, edge_index, edge_weight1, L1_gnn_W1l, L1_gnn_b1, L1_gnn_W1r, L1_gnn_W2l, L1_gnn_b2, L1_gnn_W2r, L1_gnn_W3l, L1_gnn_b3, L1_gnn_W3r), axis=-1)
    x = _layernorm(x + _L2_gnn_ref(x, src, dst, 3125, L2_gnn_W), axis=-1)
    x = _layernorm(x + _L3_gnn_ref(x, edge_attr_128, src, dst, L3_gnn_W_msg_0, L3_gnn_b_msg_0, L3_gnn_Wih_0, L3_gnn_Whh_0, L3_gnn_bih_0, L3_gnn_bhh_0, L3_gnn_W_msg_1, L3_gnn_b_msg_1, L3_gnn_Wih_1, L3_gnn_Whh_1, L3_gnn_bih_1, L3_gnn_bhh_1), axis=-1)
    return x

_drawn_inputs = setup_inputs


def setup_inputs(seed=0):
    import zlib

    import numpy as np

    out = dict(_drawn_inputs(seed))
    spreads = {'L0_gnn_pri': (1.0, 0.6),
     'L0_gnn_skip': (1.0, 0.6),
     'L1_gnn_b1': (0.0, 0.1),
     'L1_gnn_b2': (0.0, 0.1),
     'L1_gnn_b3': (0.0, 0.1),
     'L3_gnn_b_msg_0': (0.0, 0.445),
     'L3_gnn_bih_0': (0.0, 0.341),
     'L3_gnn_bhh_0': (0.0, 0.5),
     'L3_gnn_b_msg_1': (0.0, 0.271),
     'L3_gnn_bih_1': (0.0, 0.1),
     'L3_gnn_bhh_1': (0.0, 0.358)}
    factors = {}
    for name, (base, spread) in spreads.items():
        noise = np.random.default_rng([zlib.crc32(name.encode()), seed]).standard_normal(out[name].shape)
        drawn = base * np.exp(spread * noise) if base else spread * noise
        out[name] = jnp.asarray(drawn.astype(out[name].dtype))
    for name, factor in factors.items():
        out[name] = (out[name] * factor).astype(out[name].dtype)
    return out
```

```python
from contextlib import ExitStack

import concourse.bass as bass
from concourse import mybir

F32 = mybir.dt.float32
I32 = mybir.dt.int32
ALU = mybir.AluOpType
ACT = mybir.ActivationFunctionType
AX = mybir.AxisListType

P = 128
N_NODES = 3125
N_EDGES = 50000
NT = -(-N_NODES // P)
NP = NT * P
NC = 392
CB = NC // 4
S = NC + NT - 1
HEADS, HD = 8, 16
NTYPES, ETYPES, LAYERS = 3, 6, 2
U = 8
NG = S // U
SG = 16
NSG = S // SG
BIG = 1.0e30
EPS = 1e-5
assert S % (2 * U) == 0 and SG * HEADS == P and S % SG == 0

COLS = [(c, min(512, NP - c)) for c in range(0, NP, 512)]


def gnn_kernel(nc, a, out):
    ctx = ExitStack()
    with ctx:
        def sb(name, shape, dt=F32):
            return ctx.enter_context(nc.sbuf_tensor(name, shape, dt))

        def sem(name):
            return ctx.enter_context(nc.semaphore(name))

        def dram(name, shape, dt=F32):
            return nc.dram_tensor(name, shape, dt, kind="Internal").ap()

        PS = ctx.enter_context(nc.psum_tensor("PS", [P, 8 * 512], F32))

        kv_table = dram("kv_table", [ETYPES * NP, 2 * P])
        v_edges = dram("v_edges", [NG, P, U * P])
        h_table = dram("h_table", [NP, P])

        ident = sb("ident", [P, P])
        iota_row = sb("iota_row", [P, P])
        iota_steps = sb("iota_steps", [P, S])
        dst_s = sb("dst_s", [P, S])
        rel_s = sb("rel_s", [P, S])
        invalid_s = sb("invalid_s", [P, S])
        kv_index = sb("kv_index", [P, S], I32)
        src_index = sb("src_index", [P, S], I32)
        tile_s = sb("tile_s", [P, S], I32)
        chunk_s = sb("chunk_s", [P, S], I32)
        type_row = sb("type_row", [P, NP])
        xn = sb("xn", [P, NP])
        xt = sb("xt", [P, NP])
        ht = sb("ht", [P, NP])
        work = sb("work", [P, 2, NSG * P])
        agg, aggt = work[:, 0, 0:NP], work[:, 1, 0:NP]
        onehot = sb("onehot", [P, 2, U, P])
        rows = sb("rows", [P, 2, U, 2 * P])
        gather_index = sb("gather_index", [P, 2, U], I32)

        fence = sb("fence", [1, 2])
        n_sems, n_temps, stage_sems = [0], [0], []

        def temporary(scope, name, shape, dt=F32):
            n_temps[0] += 1
            return scope.enter_context(nc.sbuf_tensor(f"{name}_{n_temps[0]}", shape, dt))

        def stage_sem(name):
            n_sems[0] += 1
            stage_sems.append(nc.alloc_semaphore(name=f"{name}_{n_sems[0]}"))
            return stage_sems[-1]

        def index_fence(pool):
            pool.tensor_tensor(fence[:, 1:2], fence[:, 0:1], fence[:, 0:1], ALU.add)

        def recycle_semaphores():
            nc.clear_and_free_semaphores(stage_sems)
            stage_sems.clear()
            nc.all_engine_barrier()

        def load_constants():
            ready = stage_sem("consts")
            with nc.Block() as block:
                @block.gpsimd
                def _(pool):
                    pool.memset(ident[:, :], 0.0).then_inc(ready, 1)
                    pool.memset(fence[:, :], 0.0)
                    pool.iota(iota_row[:, :], [[1, P]], base=0, channel_multiplier=0,
                              allow_small_or_imprecise_dtypes=True)
                    pool.iota(iota_steps[:, :], [[1, S]], base=0, channel_multiplier=0,
                              allow_small_or_imprecise_dtypes=True)
                    pool.wait_ge(ready, 1)
                    pool.affine_select(out=ident[:, :], in_=ident[:, :], compare_op=ALU.not_equal, fill=1.0,
                                       base=0, pattern=[[-1, P]], channel_multiplier=1)

        def plan_steps():
            loaded, cast, first, planned, spread, made = (stage_sem(n) for n in
                                                          ("idx_loaded", "idx_cast", "tile_of", "sel", "spread", "idx"))
            chain = stage_sem("plan_chain")
            with ExitStack() as tmp:
                def tb(name, shape, dt=F32):
                    return temporary(tmp, name, shape, dt)
                raw = tb("raw", [CB, 3, 4, P], I32)
                flt = tb("flt", [CB, 4, 4, P])
                nxt = tb("nxt", [CB, 4], I32)
                begin_i = tb("begin_i", [CB, 2, 4], I32)
                begin = tb("begin", [CB, 2, 4])
                cidx = tb("cidx", [CB, 4])
                past = tb("past", [CB, 4, S])
                sel = tb("sel", [CB, 4, S])
                tilef = tb("tilef", [P, S])
                t1 = tb("t1", [P, S])
                with nc.Block() as block:
                    @block.sync
                    def _(sp):
                        for n, name in enumerate(("dst", "src", "edge_type")):
                            sp.dma_start(raw[:, n], a[name][0:NC * P].rearrange("(b c p) -> c b p", b=4, c=CB))\
                              .then_inc(loaded, 16)
                        with nc.allow_non_contiguous_dma("one element of each chunk"):
                            sp.dma_start(nxt[:, :], a["dst"][P:(NC + 1) * P]
                                         .rearrange("(b c p) -> c b p", b=4, c=CB)[:, :, 0]).then_inc(loaded, 16)

                    @block.gpsimd
                    def _(pool):
                        pool.iota(cidx[:, :], [[CB, 4]], base=0, channel_multiplier=1,
                                  allow_small_or_imprecise_dtypes=True).then_inc(planned, 1)

                    @block.vector
                    def _(dve):
                        n = 0

                        def step(ins):
                            nonlocal n
                            n += 1
                            ins.then_inc(chain, 1)
                            dve.wait_ge(chain, n)
                        dve.wait_ge(loaded, 64)
                        step(dve.tensor_single_scalar(begin_i[:, 0], raw[:, 0, :, 0], 7, ALU.logical_shift_right))
                        step(dve.tensor_single_scalar(begin_i[:, 1], nxt[:, :], 7, ALU.logical_shift_right))
                        step(dve.memset(begin_i[0:1, 0, 0:1], 0))
                        dve.wait_ge(planned, 1)
                        step(dve.tensor_copy(begin[:, :], begin_i[:, :]))
                        step(dve.tensor_tensor(begin[:, 0], begin[:, 0], cidx[:, :], ALU.add))
                        step(dve.scalar_tensor_tensor(out=begin[:, 1], in0=begin[:, 1], scalar=1.0, in1=cidx[:, :],
                                                      op0=ALU.add, op1=ALU.add))
                        for b in range(4):
                            dve.tensor_scalar(past[:, b], iota_steps[0:CB, :], begin[:, 1, b:b + 1], None,
                                              ALU.is_ge).then_inc(chain, 1)
                        n += 4
                        dve.wait_ge(chain, n)
                        for b in range(4):
                            dve.scalar_tensor_tensor(out=sel[:, b], in0=iota_steps[0:CB, :],
                                                     scalar=begin[:, 0, b:b + 1], in1=past[:, b],
                                                     op0=ALU.is_ge, op1=ALU.subtract)
                        for q in range(3):
                            dve.tensor_copy(flt[:, q], raw[:, q])
                        dve.tensor_copy(flt[:, 3], cidx[:, :][:, :, None].broadcast_to([CB, 4, P])).then_inc(cast, 1)
                        dve.wait_ge(spread, 1)
                        dq, sq, eq, cq = (PS[:, q * 512:q * 512 + S] for q in range(4))
                        n0 = n
                        dve.tensor_copy(dst_s[:, :], dq).then_inc(chain, 1)
                        dve.tensor_copy(src_index[:, :], sq).then_inc(chain, 1)
                        dve.tensor_copy(chunk_s[:, :], cq).then_inc(chain, 1)
                        dve.tensor_tensor(tilef[:, :], iota_steps[:, :], cq, ALU.subtract).then_inc(chain, 1)
                        dve.tensor_scalar(t1[:, :], eq, float(NP), None, ALU.mult).then_inc(chain, 1)
                        n = n0 + 5
                        dve.wait_ge(chain, n)
                        step(dve.tensor_tensor(kv_index[:, :], t1[:, :], sq, ALU.add))
                        step(dve.tensor_copy(tile_s[:, :], tilef[:, :]))
                        step(dve.scalar_tensor_tensor(out=rel_s[:, :], in0=tilef[:, :], scalar=-float(P),
                                                      in1=dst_s[:, :], op0=ALU.mult, op1=ALU.add))
                        step(dve.tensor_scalar(t1[:, :], rel_s[:, :], 0.0, None, ALU.is_ge))
                        step(dve.scalar_tensor_tensor(out=tilef[:, :], in0=rel_s[:, :], scalar=float(P) - 0.5,
                                                      in1=t1[:, :], op0=ALU.is_lt, op1=ALU.mult))
                        step(dve.tensor_scalar(invalid_s[:, :], tilef[:, :], 1.0, BIG, ALU.subtract, ALU.mult))

                    @block.tensor
                    def _(pe):
                        pe.wait_ge(cast, 1)
                        for q in range(4):
                            for b in range(4):
                                mm = pe.matmul(PS[:, q * 512:q * 512 + S], flt[:, q, b], sel[:, b],
                                               start=(b == 0), stop=(b == 3))
                        mm.then_inc(spread, 1)

        def transpose_blocks(dst, src, add=None):
            turned, by_dve, by_act = stage_sem("turned"), stage_sem("out_dve"), stage_sem("out_act")
            with nc.Block() as block:
                @block.tensor
                def _(pe):
                    for g, (c, w) in enumerate(COLS):
                        if g >= 4:
                            pe.wait_ge((by_dve, by_act)[g % 2], (g - 4) // 2 + 1)
                        for t in range(w // P):
                            mm = pe.transpose(PS[:, (g % 4) * 512 + t * P:(g % 4) * 512 + (t + 1) * P],
                                              src[:, c + t * P:c + (t + 1) * P], ident[:, :])
                        mm.then_inc(turned, 1)

                @block.vector
                def _(dve):
                    for g, (c, w) in enumerate(COLS):
                        if g % 2 == 0:
                            dve.wait_ge(turned, g + 1)
                            dve.tensor_copy(dst[:, c:c + w], PS[:, (g % 4) * 512:(g % 4) * 512 + w]).then_inc(by_dve, 1)

                @block.scalar
                def _(act):
                    for g, (c, w) in enumerate(COLS):
                        if g % 2 == 1:
                            act.wait_ge(turned, g + 1)
                            act.copy(dst[:, c:c + w], PS[:, (g % 4) * 512:(g % 4) * 512 + w]).then_inc(by_act, 1)

        def clear_sums(pe, zeros):
            for k in range(8):
                mm = pe.matmul(PS[:, k * 512:(k + 1) * 512], zeros[:, 0:P], zeros[:, :],
                               start=True, stop=False, skip_group_check=True)
            return mm

        def segment_sums(kind, ea=None):
            zeroed = stage_sem("zeroed")
            per = 1 if kind == "values" else U
            got = [stage_sem("rows_in0"), stage_sem("rows_in1")]
            idx_in, hot, used, weighted = (stage_sem(n) for n in ("idx_in", "hot", "used", "weighted"))
            with ExitStack() as tmp:
                zeros = temporary(tmp, "zeros", [P, 512])
                ones = temporary(tmp, "ones", [P, HEADS])
                with nc.Block() as block:
                    if kind == "gather":
                        @block.gpsimd
                        def _(pool):
                            with pool.Fori(0, NG // 2) as i:
                                for b in range(2):
                                    pool.wait_ge(used, 2 * i + b + 1)
                                    pool.tensor_copy(gather_index[:, b], src_index[:, bass.ds((2 * i + b) * U, U)])\
                                        .then_inc(idx_in, 1)
                                    pool.wait_ge(idx_in, 2 * i + b + 1)
                                    index_fence(pool)
                                    for u in range(U):
                                        pool.indirect_dma_start(
                                            rows[:, b, u, 0:P], None, h_table,
                                            bass.IndirectOffsetOnAxis(ap=gather_index[:, b, u:u + 1], axis=0)
                                        ).then_inc(got[b], 16)
                    else:
                        @block.sync
                        def _(sp):
                            with sp.Fori(0, NG // 2) as i:
                                for b in range(2):
                                    sp.wait_ge(used, 2 * i + b + 1)
                                    if kind == "values":
                                        sp.dma_start(rows[:, b, :, 0:P],
                                                     v_edges[bass.ds(2 * i + b, 1)].rearrange("g p (u f) -> p (g u) f", u=U))\
                                          .then_inc(got[b], 16)
                                    else:
                                        for u in range(U):
                                            c = sp.value_load(chunk_s[0:1, bass.ds((2 * i + b) * U + u, 1)],
                                                              min_val=0, max_val=NC - 1)
                                            sp.dma_start(rows[:, b, u, 0:P],
                                                         a["edge_attr"][bass.ds(c, 1)].rearrange("c p f -> (c p) f"))\
                                              .then_inc(got[b], 16)

                    @block.vector
                    def _(dve):
                        dve.memset(zeros[:, :], 0.0).then_inc(zeroed, 1)
                        dve.memset(ones[:, :], 1.0).then_inc(used, 2)
                        with dve.Fori(0, NG // 2) as i:
                            for b in range(2):
                                dve.wait_ge(used, 2 * i + b + 1)
                                if kind == "values":
                                    dve.wait_ge(got[b], 16 * per * (i + 1))
                                    v = rows[:, b, :, 0:P].rearrange("p u (h d) -> p u h d", h=HEADS)
                                    w = ea[:, bass.ds((2 * i + b) * U * HEADS, U * HEADS)]
                                    dve.tensor_tensor(v, v, w.rearrange("p (u h) -> p u h", h=HEADS)[:, :, :, None]
                                                      .broadcast_to([P, U, HEADS, HD]), ALU.mult)
                                dve.tensor_tensor(onehot[:, b], iota_row[:, None, :].broadcast_to([P, U, P]),
                                                  rel_s[:, bass.ds((2 * i + b) * U, U)][:, :, None]
                                                  .broadcast_to([P, U, P]), ALU.is_equal).then_inc(hot, 1)

                    @block.tensor
                    def _(pe):
                        pe.wait_ge(zeroed, 1)
                        clear_sums(pe, zeros)
                        with pe.Fori(0, NG // 2) as i:
                            for b in range(2):
                                pe.wait_ge(hot, 2 * i + b + 1)
                                pe.wait_ge(got[b], 16 * per * (i + 1))
                                for u in range(U):
                                    t = pe.value_load(tile_s[0:1, bass.ds((2 * i + b) * U + u, 1)],
                                                      min_val=0, max_val=NT - 1)
                                    mm = pe.matmul(PS[:, bass.ds(t * P, P)], onehot[:, b, u], rows[:, b, u, 0:P],
                                                   start=False, stop=False, skip_group_check=True)
                                    if kind == "values":
                                        mm = pe.matmul(PS[:, bass.ds(7 * 512 + t * HEADS, HEADS)], onehot[:, b, u],
                                                       ea[:, bass.ds(((2 * i + b) * U + u) * HEADS, HEADS)],
                                                       start=False, stop=False, skip_group_check=True)
                                    if kind == "edges":
                                        mm = pe.matmul(PS[:, bass.ds(7 * 512 + t * HEADS, HEADS)], onehot[:, b, u],
                                                       ones[:, :], start=False, stop=False, skip_group_check=True)
                                mm.then_inc(used, 1)

        def edge_means():
            segment_sums("edges")
            chain, rowed, spread = stage_sem("deg_chain"), stage_sem("deg_row"), stage_sem("deg_spread")
            with ExitStack() as tmp:
                def tb(name, shape, dt=F32):
                    return temporary(tmp, name, shape, dt)
                deg = tb("deg", [P, NT])
                low = tb("low", [P, NT])
                has = tb("has", [P, NT])
                has_row = tb("has_row", [1, NP])
                one_row = tb("one_row", [1, P])
                with nc.Block() as block:
                    @block.vector
                    def _(dve):
                        dve.memset(one_row[:, :], 1.0)
                        dve.tensor_copy(deg[:, :], PS[:, 7 * 512:7 * 512 + NT * HEADS:HEADS]).then_inc(chain, 1)
                        dve.wait_ge(chain, 1)
                        dve.tensor_scalar(low[:, :], deg[:, :], 1.0, None, ALU.max).then_inc(chain, 1)
                        dve.tensor_scalar(has[:, :], deg[:, :], 1.0, None, ALU.min).then_inc(chain, 1)
                        dve.wait_ge(chain, 3)
                        dve.reciprocal(deg_inv[:, :], low[:, :]).then_inc(chain, 1)
                        dve.wait_ge(chain, 4)
                        dve.tensor_tensor(agg[:, :].rearrange("p (t f) -> p t f", f=P),
                                          PS[:, 0:NP].rearrange("p (t f) -> p t f", f=P),
                                          deg_inv[:, :][:, :, None].broadcast_to([P, NT, P]), ALU.mult).then_inc(chain, 1)
                        for k, (c, w) in enumerate(COLS):
                            dve.wait_ge(rowed, k + 1)
                            dve.tensor_copy(has_row[:, c:c + w], PS[0:1, k * 512:k * 512 + w]).then_inc(chain, 1)
                        dve.wait_ge(spread, 1)
                        dve.tensor_copy(has_edge_row[:, :], PS[:, 0:NP])

                    @block.tensor
                    def _(pe):
                        pe.wait_ge(chain, 5)
                        for k, (c, w) in enumerate(COLS):
                            for t in range(w // P):
                                mm = pe.matmul(PS[0:1, c + t * P:c + (t + 1) * P],
                                               has[:, c // P + t:c // P + t + 1], ident[:, :], start=True, stop=True)
                            mm.then_inc(rowed, 1)
                        pe.wait_ge(chain, 5 + len(COLS))
                        for c, w in COLS:
                            mm = pe.matmul(PS[:, c:c + w], one_row[:, :], has_row[:, c:c + w], start=True, stop=True)
                        mm.then_inc(spread, 1)
            transpose_blocks(edge_mean, agg)

        def layernorm():
            chain, rooted = stage_sem("ln_chain"), stage_sem("ln_root")
            with ExitStack() as tmp:
                def tb(name, shape, dt=F32):
                    return temporary(tmp, name, shape, dt)
                stats = tb("stats", [P, NT, 6])
                mv = tb("mv", [P, NT, 2])
                var = tb("var", [P, NT])
                root = tb("root", [P, NT])
                rstd = tb("rstd", [P, NT])
                with nc.Block() as block:
                    @block.vector
                    def _(dve):
                        dve.tensor_tensor(xn[:, :], xn[:, :], agg[:, :], ALU.add).then_inc(chain, 1)
                        dve.wait_ge(chain, 1)
                        for t in range(NT):
                            ins = dve.bn_stats(stats[:, t], xn[:, t * P:(t + 1) * P])
                        ins.then_inc(chain, 1)
                        dve.wait_ge(chain, 2)
                        for t in range(NT):
                            ins = dve.bn_aggr(mv[:, t], stats[:, t])
                        ins.then_inc(chain, 1)
                        dve.wait_ge(chain, 3)
                        dve.tensor_scalar(var[:, :], mv[:, :, 1], EPS, None, ALU.add).then_inc(chain, 1)
                        dve.wait_ge(rooted, 1)
                        dve.reciprocal(rstd[:, :], root[:, :]).then_inc(chain, 1)
                        dve.wait_ge(chain, 5)
                        for t in range(NT):
                            dve.tensor_scalar(xn[:, t * P:(t + 1) * P], xn[:, t * P:(t + 1) * P],
                                              mv[:, t, 0:1], rstd[:, t:t + 1], ALU.subtract, ALU.mult)

                    @block.scalar
                    def _(act):
                        act.wait_ge(chain, 4)
                        act.activation(root[:, :], var[:, :], ACT.Sqrt).then_inc(rooted, 1)

        def store_table(src):
            stored = stage_sem("stored")
            with nc.Block() as block:
                @block.sync
                def _(sp):
                    sp.dma_start(h_table.rearrange("(t p) f -> p t f", p=P),
                                 src[:, :].rearrange("p (t f) -> p t f", f=P)).then_inc(stored, 16)
                    sp.wait_ge(stored, 16)

        def neighbour_means():
            segment_sums("gather")
            done = stage_sem("mean_out")
            with nc.Block() as block:
                @block.vector
                def _(dve):
                    dve.tensor_tensor(agg[:, :].rearrange("p (t f) -> p t f", f=P),
                                      PS[:, 0:NP].rearrange("p (t f) -> p t f", f=P),
                                      deg_inv[:, :][:, :, None].broadcast_to([P, NT, P]), ALU.mult).then_inc(done, 1)
            transpose_blocks(aggt, agg)

        def dense_pair(dst, w_self, w_mean, bias, self_t, func):
            loaded, summed, out_ = stage_sem("w_in"), stage_sem("dense"), stage_sem("dense_out")
            with ExitStack() as tmp:
                w = temporary(tmp, "w_pair", [P, 2, P])
                bcol = temporary(tmp, "b_col", [P, 1])
                with nc.Block() as block:
                    @block.sync
                    def _(sp):
                        sp.dma_start(w[:, 0], w_self).then_inc(loaded, 16)
                        sp.dma_start(w[:, 1], w_mean).then_inc(loaded, 16)
                        sp.dma_start(bcol[:, :], bias if bias is not None else a["zero_col"]).then_inc(loaded, 16)

                    @block.tensor
                    def _(pe):
                        pe.wait_ge(loaded, 48)
                        for k, (c, n) in enumerate(COLS):
                            pe.matmul(PS[:, k * 512:k * 512 + n], w[:, 0], self_t[:, c:c + n], start=True, stop=False)
                            pe.matmul(PS[:, k * 512:k * 512 + n], w[:, 1], aggt[:, c:c + n],
                                      start=False, stop=True).then_inc(summed, 1)

                    @block.scalar
                    def _(act):
                        act.wait_ge(loaded, 48)
                        for k, (c, n) in enumerate(COLS):
                            act.wait_ge(summed, k + 1)
                            act.activation(dst[:, c:c + n], PS[:, k * 512:k * 512 + n], func,
                                           bias=bcol[:, 0:1]).then_inc(out_, 1)

        def softmax_flags(fl):
            made, turned, chain = stage_sem("flag_wide"), stage_sem("flag_turned"), stage_sem("flag_chain")
            ends, ended = stage_sem("flag_ends"), stage_sem("flag_ended")
            with ExitStack() as tmp:
                def tb(name, shape, dt=F32):
                    return temporary(tmp, name, shape, dt)
                wide = work[:, 0].rearrange("p (g e) -> p g e", e=P)
                dt_ = work[:, 1].rearrange("p (g e) -> p g e", e=P)
                pick = tb("pick", [P, 2, HEADS])
                key = tb("key", [HEADS, 2, S])
                whole = tb("whole", [HEADS, S])
                with nc.Block() as block:
                    @block.vector
                    def _(dve):
                        n = 0

                        def step(ins):
                            nonlocal n
                            n += 1
                            ins.then_inc(chain, 1)
                            dve.wait_ge(chain, n)
                        dve.tensor_copy(wide[:, :, :].rearrange("p g (s h) -> p (g s) h", h=HEADS),
                                        dst_s[:, :][:, :, None].broadcast_to([P, S, HEADS])).then_inc(made, 1)
                        dve.tensor_copy(pick[:, 0], ident[:, 0:1].broadcast_to([P, HEADS]))
                        dve.tensor_copy(pick[:, 1], ident[:, P - 1:P].broadcast_to([P, HEADS])).then_inc(ends, 1)
                        dve.wait_ge(turned, 1)
                        step(dve.tensor_copy(dt_[:, :, :].rearrange("p g e -> p (g e)"), PS[:, 0:NSG * P]))
                        step(dve.memset(fl["begin"][:, :, 0:1], -BIG))
                        step(dve.memset(fl["end"][:, :, P - 1:P], -BIG))
                        dve.tensor_tensor(fl["begin"][:, :, 1:P], dt_[:, :, 1:P], dt_[:, :, 0:P - 1], ALU.not_equal)
                        dve.tensor_tensor(fl["other_first"][:, :, :], dt_[:, :, :],
                                          dt_[:, :, 0:1].broadcast_to([P, NSG, P]), ALU.not_equal)
                        step(dve.tensor_tensor(fl["other_last"][:, :, :], dt_[:, :, :],
                                               dt_[:, :, P - 1:P].broadcast_to([P, NSG, P]), ALU.not_equal))
                        step(dve.tensor_scalar(fl["end"][:, :, 0:P - 1], fl["begin"][:, :, 1:P], -BIG, None, ALU.mult))
                        for name, lo in (("begin", 1), ("other_first", 0), ("other_last", 0)):
                            step(dve.tensor_scalar(fl[name][:, :, lo:P], fl[name][:, :, lo:P], -BIG, None, ALU.mult))
                        dve.wait_ge(ended, 1)
                        step(dve.tensor_copy(key[:, :], PS[0:HEADS, 7 * 512 - 512:8 * 512]
                                             .rearrange("p (k s) -> p k s", k=2)[:, :, 0:S]))
                        step(dve.tensor_tensor(whole[:, :], key[:, 0], key[:, 1], ALU.not_equal))
                        step(dve.memset(fl["link"][:, :], 1.0))
                        step(dve.tensor_tensor(fl["link"][:, 1:S], key[:, 1, 0:S - 1], key[:, 0, 1:S], ALU.not_equal))
                        step(dve.tensor_scalar(fl["link"][:, :], fl["link"][:, :], -BIG, None, ALU.mult))
                        step(dve.tensor_scalar(whole[:, :], whole[:, :], -BIG, None, ALU.mult))
                        step(dve.tensor_tensor(fl["forward"][:, :], whole[:, :], fl["link"][:, 0:S], ALU.add))
                        step(dve.tensor_tensor(fl["backward"][:, :], whole[:, :], fl["link"][:, 1:S + 1], ALU.add))

                    @block.tensor
                    def _(pe):
                        pe.wait_ge(made, 1)
                        for g in range(NSG):
                            mm = pe.transpose(PS[:, g * P:(g + 1) * P], wide[:, g], ident[:, :])
                        mm.then_inc(turned, 1)
                        pe.wait_ge(ends, 1)
                        pe.wait_ge(chain, 1)
                        for k in range(2):
                            mm = pe.matmul(PS[0:HEADS, (6 + k) * 512:(6 + k) * 512 + S], pick[:, k], dst_s[:, :],
                                           start=True, stop=True)
                        mm.then_inc(ended, 1)

        def hgt_tables(layer, q_nodes):
            loaded = stage_sem("hgt_w")
            masked, k_done, kt_out, v_out, tab, tab_v, tab_a, stored0, stored1 = (
                stage_sem(n) for n in ("masked", "kvq", "kv_dve", "kv_act", "typed", "typed_dve", "typed_act",
                                       "tab_st0", "tab_st1"))
            stored = (stored0, stored1)
            wscaled = stage_sem("w_scaled")
            with ExitStack() as tmp:
                def tb(name, shape, dt=F32):
                    return temporary(tmp, name, shape, dt)
                wk, wv, wq = (tb(n, [P, NTYPES, P]) for n in ("wk", "wv", "wq"))
                bk, bv = (tb(n, [P, ETYPES, P]) for n in ("bk", "bv"))
                pri = tb("pri", [P, ETYPES])
                xm = work[:, 0, 0:2 * NTYPES * 512].rearrange("p (b t c) -> p b t c", b=2, t=NTYPES)
                kv = work[:, 1, 0:2 * 2 * 512].rearrange("p (b q c) -> p b q c", b=2, q=2)
                typed = rows[:, :].rearrange("p b u f -> p (b u) f")[:, 0:2 * ETYPES].rearrange("p (b e) f -> p b e f", b=2)
                with nc.Block() as block:
                    @block.sync
                    def _(sp):
                        for w, name in ((wk, "Wk"), (wv, "Wv"), (wq, "Wq")):
                            sp.dma_start(w[:, :], a[name][layer].rearrange("t i o -> i t o")).then_inc(loaded, 16)
                        for w, name in ((bk, "Watt_diag"), (bv, "Wmsg_diag")):
                            sp.dma_start(w[:, :], a[name][layer].rearrange("t i o -> i t o")).then_inc(loaded, 16)
                        sp.dma_start(pri[:, :], a["pri_rows"][layer]).then_inc(loaded, 16)
                        for t in range(NT):
                            sp.wait_ge(tab_v, t + 1)
                            sp.wait_ge(tab_a, t + 1)
                            sp.dma_start(kv_table.rearrange("(e t p) f -> t p e f", e=ETYPES, p=P)[t], typed[:, t % 2])\
                              .then_inc(stored[t % 2], 16)
                        sp.wait_ge(stored[0], 16 * ((NT + 1) // 2))
                        sp.wait_ge(stored[1], 16 * (NT // 2))

                    @block.vector
                    def _(dve):
                        dve.wait_ge(loaded, 96)
                        for e in range(ETYPES):
                            ins = dve.tensor_scalar(bk[:, e], bk[:, e], pri[:, e:e + 1], 0.25, ALU.mult, ALU.mult)
                        ins.then_inc(wscaled, 1)

                        def mask(k):
                            c, w = COLS[k]
                            if k >= 2:
                                dve.wait_ge(k_done, 2 * (k - 1))
                            for t in range(NTYPES):
                                ins = dve.scalar_tensor_tensor(out=xm[:, k % 2, t, 0:w], in0=type_row[:, c:c + w],
                                                               scalar=float(t), in1=xt[:, c:c + w],
                                                               op0=ALU.is_equal, op1=ALU.mult)
                            ins.then_inc(masked, 1)
                        mask(0)
                        for k, (c, w) in enumerate(COLS):
                            if k + 1 < len(COLS):
                                mask(k + 1)
                            dve.wait_ge(k_done, 2 * k + 1)
                            if k >= 2:
                                dve.wait_ge(tab, 4 * (k - 1))
                            dve.tensor_copy(kv[:, k % 2, 0, 0:w], PS[:, 0:w]).then_inc(kt_out, 1)
                            dve.wait_ge(k_done, 2 * k + 2)
                            dve.tensor_copy(q_nodes[:, c:c + w], PS[:, 1024:1024 + w]).then_inc(kt_out, 1)
                            for t in range(w // P):
                                n = c // P + t
                                dve.wait_ge(tab, n + 1)
                                if n >= 2:
                                    dve.wait_ge(stored[n % 2], 16 * (n // 2))
                                dve.tensor_copy(typed[:, n % 2, :, 0:P].rearrange("p (a b) f -> p a (b f)", a=2) if False else
                                                typed[:, n % 2, 0:3, 0:P], PS[:, 2048:2048 + 384].rearrange("p (e f) -> p e f", f=P))
                                dve.tensor_copy(typed[:, n % 2, 3:6, 0:P],
                                                PS[:, 2560:2560 + 384].rearrange("p (e f) -> p e f", f=P)).then_inc(tab_v, 1)

                    @block.scalar
                    def _(act):
                        for k, (c, w) in enumerate(COLS):
                            act.wait_ge(k_done, 2 * k + 1)
                            if k >= 2:
                                act.wait_ge(tab, 4 * (k - 1))
                            act.copy(kv[:, k % 2, 1, 0:w], PS[:, 512:512 + w]).then_inc(v_out, 1)
                            for t in range(w // P):
                                n = c // P + t
                                act.wait_ge(tab, n + 1)
                                if n >= 2:
                                    act.wait_ge(stored[n % 2], 16 * (n // 2))
                                act.copy(typed[:, n % 2, 0:3, P:2 * P], PS[:, 3072:3072 + 384].rearrange("p (e f) -> p e f", f=P))
                                act.copy(typed[:, n % 2, 3:6, P:2 * P],
                                         PS[:, 3584:3584 + 384].rearrange("p (e f) -> p e f", f=P)).then_inc(tab_a, 1)

                    @block.tensor
                    def _(pe):
                        pe.wait_ge(loaded, 96)
                        pe.wait_ge(wscaled, 1)
                        for k, (c, w) in enumerate(COLS):
                            pe.wait_ge(masked, k + 1)
                            if k >= 1:
                                pe.wait_ge(kt_out, 2 * k)
                                pe.wait_ge(v_out, k)
                            for q, wt in ((0, wk), (1, wv)):
                                for t in range(NTYPES):
                                    mm = pe.matmul(PS[:, q * 512:q * 512 + w], wt[:, t], xm[:, k % 2, t, 0:w],
                                                   start=(t == 0), stop=(t == NTYPES - 1))
                            mm.then_inc(k_done, 1)
                            for m in range(w // P):
                                for t in range(NTYPES):
                                    mm = pe.matmul(PS[:, 1024 + m * P:1024 + (m + 1) * P], xm[:, k % 2, t, m * P:(m + 1) * P],
                                                   wq[:, t], start=(t == 0), stop=(t == NTYPES - 1))
                            mm.then_inc(k_done, 1)
                            pe.wait_ge(kt_out, 2 * k + 1)
                            pe.wait_ge(v_out, k + 1)
                            for m in range(w // P):
                                n = c // P + m
                                if n >= 1:
                                    pe.wait_ge(tab_v, n)
                                    pe.wait_ge(tab_a, n)
                                for q, bw in ((0, bk), (1, bv)):
                                    for half in range(2):
                                        at = 2048 + q * 1024 + half * 512
                                        mm = pe.matmul(PS[:, at:at + 384], kv[:, k % 2, q, m * P:(m + 1) * P],
                                                       bw[:, 3 * half:3 * half + 3].rearrange("p e f -> p (e f)"),
                                                       start=True, stop=True)
                                mm.then_inc(tab, 1)

        def hgt_scores(q_nodes, scores):
            got = [stage_sem("kv_in0"), stage_sem("kv_in1")]
            spilled = [stage_sem("spill0"), stage_sem("spill1")]
            idx_in, hot, hot_t, hot_c, qe, used = (
                stage_sem(n) for n in ("idx_in", "hot", "hot_t", "hot_c", "qe", "used"))
            prod_done = stage_sem("prod")
            with ExitStack() as tmp:
                hot_sb = temporary(tmp, "hot_sb", [P, 2, U * P])
                prod = temporary(tmp, "prod", [P, U * P])
                with nc.Block() as block:
                    @block.gpsimd
                    def _(pool):
                        with pool.Fori(0, NG // 2) as i:
                            for b in range(2):
                                pool.wait_ge(used, 2 * i + b + 1)
                                pool.wait_ge(spilled[b], 16 * (i + 1))
                                pool.tensor_copy(gather_index[:, b], kv_index[:, bass.ds((2 * i + b) * U, U)])\
                                    .then_inc(idx_in, 1)
                                pool.wait_ge(idx_in, 2 * i + b + 1)
                                index_fence(pool)
                                for u in range(U):
                                    pool.indirect_dma_start(
                                        rows[:, b, u], None, kv_table,
                                        bass.IndirectOffsetOnAxis(ap=gather_index[:, b, u:u + 1], axis=0)
                                    ).then_inc(got[b], 16)

                    @block.sync
                    def _(sp):
                        with sp.Fori(0, NG // 2) as i:
                            for b in range(2):
                                sp.wait_ge(got[b], 16 * U * (i + 1))
                                sp.dma_start(v_edges[bass.ds(2 * i + b, 1)].rearrange("g p (u f) -> p (g u) f", u=U),
                                             rows[:, b, :, P:2 * P]).then_inc(spilled[b], 16)
                        for b in range(2):
                            sp.wait_ge(spilled[b], 16 * (NG // 2 + 1))

                    @block.vector
                    def _(dve):
                        for s_, credit in ((used, 2), (hot_t, 1), (spilled[0], 16), (spilled[1], 16)):
                            dve.nop().then_inc(s_, credit)

                        def make_hot(group, b):
                            dve.tensor_tensor(onehot[:, b], iota_row[:, None, :].broadcast_to([P, U, P]),
                                              rel_s[:, bass.ds(group * U, U)][:, :, None].broadcast_to([P, U, P]),
                                              ALU.is_equal).then_inc(hot, 1)
                        with dve.Fori(0, NG // 2) as i:
                            for b in range(2):
                                g = 2 * i + b
                                dve.wait_ge(hot_t, g + 1)
                                make_hot(g, b)
                                dve.wait_ge(qe, g + 1)
                                dve.wait_ge(got[b], 16 * U * (i + 1))
                                dve.tensor_tensor(prod[:, :].rearrange("p (u f) -> p u f", f=P), rows[:, b, :, 0:P],
                                                  PS[:, (4 + 2 * b) * 512:(6 + 2 * b) * 512].rearrange("p (u f) -> p u f", f=P),
                                                  ALU.mult).then_inc(prod_done, 1)
                                dve.wait_ge(prod_done, g + 1)
                                dve.tensor_reduce(scores[:, bass.ds(g * U * HEADS, U * HEADS)],
                                                  prod[:, :].rearrange("p (a d) -> p a d", d=HD), AX.X, ALU.add)\
                                   .then_inc(used, 1)

                    @block.scalar
                    def _(act):
                        with act.Fori(0, NG // 2) as i:
                            for b in range(2):
                                act.wait_ge(hot_t, 2 * i + b + 2)
                                act.copy(hot_sb[:, b], PS[:, 2 * b * 512:(2 * b + 2) * 512]).then_inc(hot_c, 1)

                    @block.tensor
                    def _(pe):
                        with pe.Fori(0, NG // 2) as i:
                            for b in range(2):
                                g = 2 * i + b
                                pe.wait_ge(hot, g + 1)
                                for u in range(U):
                                    mm = pe.transpose(PS[:, 2 * b * 512 + u * P:2 * b * 512 + (u + 1) * P],
                                                      onehot[:, b, u], ident[:, :])
                                mm.then_inc(hot_t, 1)
                                pe.wait_ge(used, g + 1)
                                pe.wait_ge(hot_c, g + 1)
                                for u in range(U):
                                    t = pe.value_load(tile_s[0:1, bass.ds(g * U + u, 1)], min_val=0, max_val=NT - 1)
                                    mm = pe.matmul(PS[:, (4 + 2 * b) * 512 + u * P:(4 + 2 * b) * 512 + (u + 1) * P],
                                                   hot_sb[:, b, u * P:(u + 1) * P], q_nodes[:, bass.ds(t * P, P)],
                                                   start=True, stop=True)
                                mm.then_inc(qe, 1)

        def edge_softmax(scores, fl, head_rows):
            masked, turned, chain, ends, back, exped, returned = (
                stage_sem(n) for n in ("sm_masked", "sm_turned", "sm_chain", "sm_ends", "sm_back", "sm_exp", "sm_ret"))
            with ExitStack() as tmp:
                def tb(name, shape, dt=F32):
                    return temporary(tmp, name, shape, dt)
                st = work[:, 0].rearrange("p (g e) -> p g e", e=P)
                run = work[:, 1].rearrange("p (g e) -> p g e", e=P)
                top = rows[:, :].rearrange("p b u f -> p (b u f)")[:, 0:NSG * P].rearrange("p (g e) -> p g e", e=P)
                first_last = tb("first_last", [HEADS, 2, S])
                carry = tb("carry", [HEADS, 2, S])
                into = tb("into", [HEADS, 2, S])
                into_t = tb("into_t", [P, 2, NSG])

                def flat(x):
                    return x[:, :, :].rearrange("p g e -> p (g e)")
                with nc.Block() as block:
                    @block.vector
                    def _(dve):
                        n = 0

                        def step(ins):
                            nonlocal n
                            n += 1
                            ins.then_inc(chain, 1)
                            dve.wait_ge(chain, n)
                        dve.tensor_tensor(scores[:, :].rearrange("p (s h) -> p s h", h=HEADS),
                                          scores[:, :].rearrange("p (s h) -> p s h", h=HEADS),
                                          invalid_s[:, :][:, :, None].broadcast_to([P, S, HEADS]), ALU.add)\
                            .then_inc(masked, 1)
                        dve.wait_ge(turned, 1)
                        step(dve.tensor_copy(flat(st), PS[:, 0:NSG * P]))
                        step(dve.tensor_tensor_scan(flat(run), flat(fl["begin"]), flat(st), -BIG, ALU.add, ALU.max))
                        step(dve.tensor_tensor_scan(flat(top)[:, ::-1], flat(fl["end"])[:, ::-1], flat(run)[:, ::-1],
                                                    -BIG, ALU.add, ALU.max))
                        dve.wait_ge(ends, 1)
                        step(dve.tensor_copy(first_last[:, :],
                                             PS[0:HEADS, 0:1024].rearrange("p (k s) -> p k s", k=2)[:, :, 0:S]))
                        step(dve.tensor_tensor_scan(carry[:, 0], fl["forward"][:, :], first_last[:, 1], -BIG,
                                                    ALU.add, ALU.max))
                        step(dve.tensor_tensor_scan(carry[:, 1, ::-1], fl["backward"][:, ::-1], first_last[:, 0, ::-1],
                                                    -BIG, ALU.add, ALU.max))
                        step(dve.memset(into[:, :], -BIG))
                        step(dve.tensor_tensor(into[:, 0, 1:S], carry[:, 0, 0:S - 1], fl["link"][:, 1:S], ALU.add))
                        step(dve.tensor_tensor(into[:, 1, 0:S - 1], carry[:, 1, 1:S], fl["link"][:, 1:S], ALU.add))
                        dve.wait_ge(back, 1)
                        step(dve.tensor_copy(into_t[:, :], PS[:, 1024:1024 + 2 * NSG].rearrange("p (k g) -> p k g", k=2)))
                        for k, other in ((0, "other_first"), (1, "other_last")):
                            step(dve.tensor_tensor(run[:, :, :], fl[other][:, :, :],
                                                   into_t[:, k][:, :, None].broadcast_to([P, NSG, P]), ALU.add))
                            step(dve.tensor_tensor(top[:, :, :], top[:, :, :], run[:, :, :], ALU.max))
                        step(dve.tensor_tensor(st[:, :, :], st[:, :, :], top[:, :, :], ALU.subtract))
                        dve.wait_ge(returned, 1)
                        dve.tensor_copy(scores[:, :], PS[:, 0:NSG * P])

                    @block.scalar
                    def _(act):
                        act.wait_ge(chain, 15)
                        act.activation(flat(st), flat(st), ACT.Exp).then_inc(exped, 1)

                    @block.tensor
                    def _(pe):
                        pe.wait_ge(masked, 1)
                        for g in range(NSG):
                            mm = pe.transpose(PS[:, g * P:(g + 1) * P], scores[:, g * P:(g + 1) * P], ident[:, :])
                        mm.then_inc(turned, 1)
                        pe.wait_ge(chain, 3)
                        for k, at in ((0, 0), (1, P - 1)):
                            for s in range(SG):
                                mm = pe.matmul(PS[0:HEADS, k * 512 + s:k * 512 + S:SG], ident[:, s * HEADS:(s + 1) * HEADS],
                                               top[:, :, at], start=True, stop=True, skip_group_check=True)
                        mm.then_inc(ends, 1)
                        pe.wait_ge(chain, 9)
                        for k in range(2):
                            for s in range(SG):
                                mm = pe.matmul(PS[:, 1024 + k * NSG:1024 + (k + 1) * NSG], head_rows[:, s], into[:, k, s::SG],
                                               start=(s == 0), stop=(s == SG - 1))
                        mm.then_inc(back, 1)
                        pe.wait_ge(exped, 1)
                        for g in range(NSG):
                            mm = pe.transpose(PS[:, g * P:(g + 1) * P], st[:, g], ident[:, :])
                        mm.then_inc(returned, 1)

        def make_head_rows(head_rows):
            turned, copied = stage_sem("hr_t"), stage_sem("hr_c")
            with nc.Block() as block:
                @block.tensor
                def _(pe):
                    for s in range(SG):
                        mm = pe.matmul(PS[0:HEADS, s * P:(s + 1) * P], ident[:, s * HEADS:(s + 1) * HEADS], ident[:, :],
                                       start=True, stop=True)
                    mm.then_inc(turned, 1)

                @block.vector
                def _(dve):
                    dve.wait_ge(turned, 1)
                    dve.tensor_copy(head_rows[:, :].rearrange("p s c -> p (s c)"), PS[0:HEADS, 0:SG * P])

        def hgt_output(layer, alpha_row, base_t):
            chain = stage_sem("ho_chain")
            with ExitStack() as tmp:
                rz = temporary(tmp, "rz", [P, NT * HEADS])
                with nc.Block() as block:
                    @block.vector
                    def _(dve):
                        dve.tensor_scalar(rz[:, :], PS[:, 7 * 512:7 * 512 + NT * HEADS], 1e-30, None, ALU.max).then_inc(chain, 1)
                        dve.wait_ge(chain, 1)
                        dve.reciprocal(rz[:, :], rz[:, :]).then_inc(chain, 1)
                        dve.wait_ge(chain, 2)
                        dve.tensor_tensor(agg[:, :].rearrange("p (a d) -> p a d", d=HD),
                                          PS[:, 0:NP].rearrange("p (a d) -> p a d", d=HD),
                                          rz[:, :][:, :, None].broadcast_to([P, NT * HEADS, HD]), ALU.mult)
            transpose_blocks(aggt, agg)
            loaded, masked, summed, done = (stage_sem(n) for n in ("wa_in", "wa_masked", "wa_sum", "wa_done"))
            ch2 = stage_sem("wa_chain")
            with ExitStack() as tmp:
                wa = temporary(tmp, "wa", [P, NTYPES, P])
                hm = rows[:, :].rearrange("p b u f -> p (b u f)")[:, 0:2 * NTYPES * 512]\
                    .rearrange("p (b t c) -> p b t c", b=2, t=NTYPES)
                diff = temporary(tmp, "diff", [P, 512])
                with nc.Block() as block:
                    @block.sync
                    def _(sp):
                        sp.dma_start(wa[:, :], a["Wa"][layer].rearrange("t i o -> i t o")).then_inc(loaded, 16)

                    @block.vector
                    def _(dve):
                        n = 0

                        def step(ins):
                            nonlocal n
                            n += 1
                            ins.then_inc(ch2, 1)
                            dve.wait_ge(ch2, n)

                        def mask(k):
                            c, w = COLS[k]
                            if k >= 2:
                                dve.wait_ge(summed, k - 1)
                            for t in range(NTYPES):
                                ins = dve.scalar_tensor_tensor(out=hm[:, k % 2, t, 0:w], in0=type_row[:, c:c + w],
                                                               scalar=float(t), in1=aggt[:, c:c + w],
                                                               op0=ALU.is_equal, op1=ALU.mult)
                            ins.then_inc(masked, 1)
                        mask(0)
                        for k, (c, w) in enumerate(COLS):
                            if k + 1 < len(COLS):
                                mask(k + 1)
                            dve.wait_ge(summed, k + 1)
                            step(dve.tensor_tensor(diff[:, 0:w], PS[:, k * 512:k * 512 + w], base_t[:, c:c + w], ALU.subtract))
                            step(dve.tensor_tensor(diff[:, 0:w], diff[:, 0:w], alpha_row[:, c:c + w], ALU.mult))
                            step(dve.tensor_tensor(base_t[:, c:c + w], base_t[:, c:c + w], diff[:, 0:w], ALU.add))

                    @block.tensor
                    def _(pe):
                        pe.wait_ge(loaded, 16)
                        for k, (c, w) in enumerate(COLS):
                            pe.wait_ge(masked, k + 1)
                            for t in range(NTYPES):
                                mm = pe.matmul(PS[:, k * 512:k * 512 + w], wa[:, t], hm[:, k % 2, t, 0:w],
                                               start=(t == 0), stop=(t == NTYPES - 1))
                            mm.then_inc(summed, 1)

        def alphas(layer, alpha_row):
            loaded, chain, sig = stage_sem("skip_in"), stage_sem("al_chain"), stage_sem("al_sig")
            with ExitStack() as tmp:
                sk = temporary(tmp, "sk", [P, NTYPES])
                al = temporary(tmp, "al", [P, NTYPES])
                part = work[:, 0, 0:NP]
                with nc.Block() as block:
                    @block.sync
                    def _(sp):
                        sp.dma_start(sk[:, :], a["skip"][layer:layer + 1, :].broadcast_to([P, NTYPES])).then_inc(loaded, 16)

                    @block.scalar
                    def _(act):
                        act.wait_ge(loaded, 16)
                        act.activation(al[:, :], sk[:, :], ACT.Sigmoid).then_inc(sig, 1)

                    @block.vector
                    def _(dve):
                        dve.wait_ge(sig, 1)
                        dve.tensor_scalar(alpha_row[:, :], type_row[:, :], 0.0, al[:, 0:1], ALU.is_equal, ALU.mult).then_inc(chain, 1)
                        for t in range(1, NTYPES):
                            dve.wait_ge(chain, 2 * t - 1)
                            dve.tensor_scalar(part[:, :], type_row[:, :], float(t), al[:, t:t + 1],
                                              ALU.is_equal, ALU.mult).then_inc(chain, 1)
                            dve.wait_ge(chain, 2 * t)
                            dve.tensor_tensor(alpha_row[:, :], alpha_row[:, :], part[:, :], ALU.add).then_inc(chain, 1)

        def load_nodes():
            loaded, cast = stage_sem("x_in"), stage_sem("type_cast")
            with ExitStack() as tmp:
                ti = tmp.enter_context(nc.sbuf_tensor("type_i", [P, NP], I32))
                with nc.Block() as block:
                    @block.sync
                    def _(sp):
                        sp.dma_start(xn[:, :].rearrange("p (t f) -> p t f", f=P),
                                     a["x"].rearrange("(t p) f -> p t f", p=P)).then_inc(loaded, 16)
                        sp.dma_start(ti[:, :], a["node_type"][None, :].broadcast_to([P, NP])).then_inc(cast, 16)
                        sp.wait_ge(loaded, 16)

                    @block.vector
                    def _(dve):
                        dve.wait_ge(cast, 16)
                        dve.tensor_copy(type_row[:, :], ti[:, :])

        def gru(n, h):
            loaded, msg, msg_out, gates, r_z, hn_b, tanh_in, tanh_out, done = (
                stage_sem(x) for x in ("gru_w", "msg", "msg_out", "gates", "r_z", "hn_b", "tin", "tout", "gdone"))
            chain = stage_sem("gru_chain")
            with ExitStack() as tmp:
                def tb(name, shape, dt=F32):
                    return temporary(tmp, name, shape, dt)
                wm = tb("wm", [P, 3, 2 * P])
                wi = tb("wi", [P, 2, 3 * P])
                wh = tb("wh", [P, 3 * P])
                bm = tb("bm", [P, 2])
                bi, bh = tb("bi", [P, 3]), tb("bh", [P, 3])
                bsum = tb("bsum", [P, 3])
                at = tb("at", [P, 2, 512])
                r, z, hn, nn = (tb(x, [P, 512]) for x in ("r", "z", "hn", "nn"))
                bank = [PS[:, k * 512:(k + 1) * 512] for k in range(6)]
                with nc.Block() as block:
                    @block.sync
                    def _(sp):
                        sp.dma_start(wm[:, :], a[f"W_msg_{n}"].rearrange("(k i) o -> i k o", k=3)).then_inc(loaded, 16)
                        sp.dma_start(wi[:, :], a[f"Wih_{n}"].rearrange("(k i) o -> i k o", k=2)).then_inc(loaded, 16)
                        sp.dma_start(wh[:, :], a[f"Whh_{n}"]).then_inc(loaded, 16)
                        for t, name in ((bm, "b_msg"), (bi, "bih"), (bh, "bhh")):
                            sp.dma_start(t[:, :], a[f"{name}_{n}"]).then_inc(loaded, 16)

                    @block.vector
                    def _(dve):
                        m = 0

                        def step(ins):
                            nonlocal m
                            m += 1
                            ins.then_inc(chain, 1)
                            dve.wait_ge(chain, m)
                        dve.wait_ge(loaded, 96)
                        step(dve.tensor_tensor(bsum[:, :], bi[:, :], bh[:, :], ALU.add))
                        for k, (c, w) in enumerate(COLS):
                            dve.wait_ge(msg, k + 1)
                            for o in range(2):
                                ins = dve.scalar_tensor_tensor(out=at[:, o, 0:w], in0=bank[o][:, 0:w], scalar=bm[:, o:o + 1],
                                                               in1=has_edge_row[:, c:c + w], op0=ALU.add, op1=ALU.mult)
                            ins.then_inc(msg_out, 1)
                            dve.wait_ge(r_z, k + 1)
                            step(dve.tensor_tensor(hn[:, 0:w], hn[:, 0:w], r[:, 0:w], ALU.mult))
                            dve.tensor_tensor(hn[:, 0:w], hn[:, 0:w], bank[4][:, 0:w], ALU.add).then_inc(tanh_in, 1)
                            dve.wait_ge(tanh_out, k + 1)
                            step(dve.tensor_tensor(hn[:, 0:w], h[:, c:c + w], nn[:, 0:w], ALU.subtract))
                            step(dve.tensor_tensor(hn[:, 0:w], hn[:, 0:w], z[:, 0:w], ALU.mult))
                            dve.tensor_tensor(h[:, c:c + w], hn[:, 0:w], nn[:, 0:w], ALU.add).then_inc(done, 1)

                    @block.scalar
                    def _(act):
                        act.wait_ge(loaded, 96)
                        act.wait_ge(chain, 1)
                        for k, (c, w) in enumerate(COLS):
                            act.wait_ge(gates, k + 1)
                            if k:
                                act.wait_ge(done, k)
                            act.activation(r[:, 0:w], bank[2][:, 0:w], ACT.Sigmoid, bias=bsum[:, 0:1])
                            act.activation(z[:, 0:w], bank[3][:, 0:w], ACT.Sigmoid, bias=bsum[:, 1:2])
                            act.activation(hn[:, 0:w], bank[5][:, 0:w], ACT.Identity, bias=bh[:, 2:3]).then_inc(r_z, 1)
                            act.wait_ge(tanh_in, k + 1)
                            act.activation(nn[:, 0:w], hn[:, 0:w], ACT.Tanh, bias=bi[:, 2:3]).then_inc(tanh_out, 1)

                    @block.tensor
                    def _(pe):
                        pe.wait_ge(loaded, 96)
                        for k, (c, w) in enumerate(COLS):
                            if k:
                                pe.wait_ge(msg_out, k)
                            for o in range(2):
                                for j, x in enumerate((h, aggt, edge_mean)):
                                    mm = pe.matmul(bank[o][:, 0:w], wm[:, j, o * P:(o + 1) * P], x[:, c:c + w],
                                                   start=(j == 0), stop=(j == 2))
                            mm.then_inc(msg, 1)
                            pe.wait_ge(msg_out, k + 1)
                            if k:
                                pe.wait_ge(tanh_in, k)
                            for gate in range(3):
                                for j in range(2):
                                    pe.matmul(bank[2 + gate][:, 0:w], wi[:, j, gate * P:(gate + 1) * P], at[:, j, 0:w],
                                              start=(j == 0), stop=(gate == 2 and j == 1))
                                mm = pe.matmul(bank[2 + gate + (gate == 2)][:, 0:w], wh[:, gate * P:(gate + 1) * P],
                                               h[:, c:c + w], start=(gate == 2), stop=True)
                            mm.then_inc(gates, 1)

        def add_out():
            stored = stage_sem("out_stored")
            full = N_NODES // P
            with nc.Block() as block:
                @block.sync
                def _(sp):
                    sp.dma_start(out[0:full * P].rearrange("(t p) f -> p t f", p=P),
                                 xn[:, 0:full * P].rearrange("p (t f) -> p t f", f=P)).then_inc(stored, 16)
                    sp.dma_start(out[full * P:N_NODES], xn[0:N_NODES - full * P, full * P:full * P + P]).then_inc(stored, 16)
                    sp.wait_ge(stored, 32)

        load_constants()
        plan_steps()
        load_nodes()
        with ExitStack() as hgt:
            def tb(name, shape, dt=F32):
                return temporary(hgt, name, shape, dt)
            head_rows = tb("head_rows", [HEADS, SG, P])
            make_head_rows(head_rows)
            fl = {n: tb(f"fl_{n}", [P, NSG, P]) for n in ("begin", "end", "other_first", "other_last")}
            fl["link"] = tb("fl_link", [HEADS, S + 1])
            fl["forward"], fl["backward"] = tb("fl_fwd", [HEADS, S]), tb("fl_bwd", [HEADS, S])
            softmax_flags(fl)
            transpose_blocks(xt, xn)
            for layer in range(LAYERS):
                hgt_tables(layer, ht)
                scores = tb(f"scores{layer}", [P, S * HEADS]) if layer == 0 else scores
                hgt_scores(ht, scores)
                edge_softmax(scores, fl, head_rows)
                segment_sums("values", scores)
                alphas(layer, ht)
                hgt_output(layer, ht, xt)
                recycle_semaphores()
        transpose_blocks(agg, xt)
        layernorm()

        has_edge_row = sb("has_edge_row", [P, NP])
        deg_inv = sb("deg_inv", [P, NT])
        edge_mean = sb("edge_mean", [P, NP])
        edge_means()

        transpose_blocks(xt, xn)
        store_table(xn)
        for n in (1, 2, 3):
            neighbour_means()
            dense_pair(ht, a[f"W{n}r"], a[f"W{n}l"], a[f"b{n}"], xt if n == 1 else ht, ACT.Relu if n < 3 else ACT.Identity)
            transpose_blocks(agg, ht)
            if n < 3:
                store_table(agg)
        layernorm()

        recycle_semaphores()

        transpose_blocks(xt, xn)
        store_table(xn)
        neighbour_means()
        dense_pair(ht, a["W_cat"][0:P], a["W_cat"][P:2 * P], None, xt, ACT.Relu)
        transpose_blocks(agg, ht)
        layernorm()

        transpose_blocks(ht, xn)
        store_table(xn)
        for n in range(2):
            neighbour_means()
            gru(n, ht)
            transpose_blocks(agg, ht)
            if n == 0:
                store_table(agg)
        layernorm()
        add_out()
        nc.clear_and_free_semaphores(stage_sems)


def kernel(**inputs):
    import numpy as np
    import concourse.bacc as bacc
    from concourse import mybir as mb
    from concourse.bass_utils import run_bass_kernel_spmd

    v = {k: np.asarray(x) for k, x in inputs.items()}

    def padded(x, n, fill):
        return np.concatenate([x, np.full((n - x.shape[0],) + x.shape[1:], fill, x.dtype)])

    def t(x):
        return np.ascontiguousarray(x.T)

    def diagonal(w):
        o = np.zeros((LAYERS, ETYPES, P, P), w.dtype)
        for h in range(HEADS):
            o[:, :, h * HD:(h + 1) * HD, h * HD:(h + 1) * HD] = w[:, h]
        return o

    edge_attr = padded(v["edge_attr_128"], NC * P, 0).reshape(NC, P, P)
    arrays = {
        "x": padded(v["x"], NP, 0),
        "dst": padded(v["dst"], (NC + 1) * P, NP - 1),
        "src": padded(v["src"], NC * P, 0),
        "edge_type": padded(v["edge_type_6"], NC * P, 0),
        "edge_attr": edge_attr,
        "node_type": padded(v["node_type_3"], NP, 0),
        "Wk": v["L0_gnn_Wk"], "Wq": v["L0_gnn_Wq"], "Wv": v["L0_gnn_Wv"], "Wa": v["L0_gnn_Wa"],
        "Watt_diag": diagonal(v["L0_gnn_Watt"]), "Wmsg_diag": diagonal(v["L0_gnn_Wmsg"]),
        "pri_rows": np.ascontiguousarray(np.repeat(v["L0_gnn_pri"], HD, axis=1)),
        "skip": v["L0_gnn_skip"],
        "zero_col": np.zeros((P, 1), np.float32),
        "W_cat": t(v["L2_gnn_W"]),
    }
    for n in (1, 2, 3):
        arrays[f"W{n}l"], arrays[f"W{n}r"] = t(v[f"L1_gnn_W{n}l"]), t(v[f"L1_gnn_W{n}r"])
        arrays[f"b{n}"] = v[f"L1_gnn_b{n}"].reshape(P, 1)
    for n in range(2):
        for w in ("W_msg", "Wih", "Whh"):
            arrays[f"{w}_{n}"] = t(v[f"L3_gnn_{w}_{n}"])
        for b in ("b_msg", "bih", "bhh"):
            arrays[f"{b}_{n}"] = t(v[f"L3_gnn_{b}_{n}"].reshape(-1, P))

    nc = bacc.Bacc("TRN2", target_bir_lowering=False, num_devices=1)
    arrays = {f"in_{k}": np.ascontiguousarray(x) for k, x in arrays.items()}
    aps = {k[3:]: nc.dram_tensor(k, x.shape, mb.dt.from_np(x.dtype), kind="ExternalInput").ap()
           for k, x in arrays.items()}
    out = nc.dram_tensor("out_0", (N_NODES, P), mb.dt.from_np(np.dtype("float32")), kind="ExternalOutput").ap()
    gnn_kernel(nc, aps, out)
    r = run_bass_kernel_spmd(nc, [arrays], core_ids=[0])
    return r.results[0]["out_0"]
```
